# Optimizing a Trainium2 kernel written in Bass

```python
import numpy as np
import jax
import jax.numpy as jnp

def _softmax(x, axis=-1):
    return jax.nn.softmax(x, axis=axis)
def _gelu(x):
    return jax.nn.gelu(x, approximate=True)
def _silu(x):
    return jax.nn.silu(x)
def _sigmoid(x):
    return jax.nn.sigmoid(x)
def _layernorm(x, axis=-1, eps=1e-5):
    m = jnp.mean(x, axis=axis, keepdims=True)
    v = jnp.var(x, axis=axis, keepdims=True)
    return (x - m) / jnp.sqrt(v + eps)
def _scatter_add(tgt, idx, src, axis=0):
    return tgt.at[idx].add(src)
def _segment_sum(src, seg, n):
    return jax.ops.segment_sum(src, seg, n)

kernel_name = 'mk_conv_preact_d1_conv_nchw512_1f59f2'

def setup_inputs(seed: int = 0):
    np.random.seed(seed)
    _w = jnp.asarray
    def _rec_inputs():
        import jax
        import jax.numpy as jnp
        _gk = jax.random.key(seed)
        x = -8.268e-05 + 0.9999 * jax.random.normal(jax.random.fold_in(_gk, 1), (32, 512, 56, 56), jnp.float32)
        return x
    x = _rec_inputs()
    def _L0_conv_setup():
        import jax, jax.numpy as jnp
        import numpy as np
        key = jax.random.key(seed)
        ks = jax.random.split(key, 7)
        N, C_in, H, W = (32, 512, 56, 56)
        C_sq, C_e1, C_e3 = (64, 256, 256)
        return {'x': jax.random.normal(ks[0], (N, C_in, H, W), dtype=jnp.float32), 'squeeze_w': jax.random.normal(ks[1], (C_sq, C_in), dtype=jnp.float32) * 0.05, 'squeeze_b': jax.random.normal(ks[2], (C_sq,), dtype=jnp.float32) * 0.05, 'expand1x1_w': jax.random.normal(ks[3], (C_e1, C_sq), dtype=jnp.float32) * 0.05, 'expand1x1_b': jax.random.normal(ks[4], (C_e1,), dtype=jnp.float32) * 0.05, 'expand3x3_w': jax.random.normal(ks[5], (C_e3, C_sq, 3, 3), dtype=jnp.float32) * 0.05, 'expand3x3_b': jax.random.normal(ks[6], (C_e3,), dtype=jnp.float32) * 0.05}
    _L0_conv_all = _L0_conv_setup()
    _L0_conv_in = {k: v for k, v in _L0_conv_all.items() if k in ('squeeze_w', 'squeeze_b', 'expand1x1_w', 'expand1x1_b', 'expand3x3_w', 'expand3x3_b', )}
    del _L0_conv_all

    return {
        "x": x,
        "L0_conv_squeeze_w": _L0_conv_in["squeeze_w"],
        "L0_conv_squeeze_b": _L0_conv_in["squeeze_b"],
        "L0_conv_expand1x1_w": _L0_conv_in["expand1x1_w"],
        "L0_conv_expand1x1_b": _L0_conv_in["expand1x1_b"],
        "L0_conv_expand3x3_w": _L0_conv_in["expand3x3_w"],
        "L0_conv_expand3x3_b": _L0_conv_in["expand3x3_b"],
    }

def reference(x, L0_conv_squeeze_w, L0_conv_squeeze_b, L0_conv_expand1x1_w, L0_conv_expand1x1_b, L0_conv_expand3x3_w, L0_conv_expand3x3_b):
    import jax
    import jax.numpy as jnp
    def _L0_conv_ref(x, squeeze_w, squeeze_b, expand1x1_w, expand1x1_b, expand3x3_w, expand3x3_b):
        import jax, jax.numpy as jnp
        import numpy as np
        s = jax.nn.relu(jnp.einsum('oc,nchw->nohw', squeeze_w, x) + squeeze_b[None, :, None, None])
        e1 = jax.nn.relu(jnp.einsum('oc,nchw->nohw', expand1x1_w, s) + expand1x1_b[None, :, None, None])
        e3 = jax.lax.conv_general_dilated(s, expand3x3_w, window_strides=(1, 1), padding=((1, 1), (1, 1)), dimension_numbers=('NCHW', 'OIHW', 'NCHW'))
        e3 = jax.nn.relu(e3 + expand3x3_b[None, :, None, None])
        return jnp.concatenate([e1, e3], axis=1)

    def _gn(v, G=32, eps=1e-5):
        B_, C_, H_, W_ = v.shape
        g = v.reshape(B_, G, C_ // G, H_, W_)
        m = jnp.mean(g, axis=(2, 3, 4), keepdims=True)
        s = jnp.var(g, axis=(2, 3, 4), keepdims=True)
        return ((g - m) / jnp.sqrt(s + eps)).reshape(v.shape)

    def _ln_c(v, eps=1e-6):
        m = jnp.mean(v, axis=1, keepdims=True)
        s = jnp.var(v, axis=1, keepdims=True)
        return (v - m) / jnp.sqrt(s + eps)

    def _ln_t(v, eps=1e-5):
        m = jnp.mean(v, axis=-1, keepdims=True)
        s = jnp.var(v, axis=-1, keepdims=True)
        return (v - m) / jnp.sqrt(s + eps)

    def _to_tokens(v):
        B_, C_, H_, W_ = v.shape
        return v.reshape(B_, C_, H_ * W_).transpose(0, 2, 1)
    def _from_tokens(t, like):
        B_, C_, H_, W_ = like.shape
        return t.transpose(0, 2, 1).reshape(B_, C_, H_, W_)

    x = x + _L0_conv_ref(_gn(x), L0_conv_squeeze_w, L0_conv_squeeze_b, L0_conv_expand1x1_w, L0_conv_expand1x1_b, L0_conv_expand3x3_w, L0_conv_expand3x3_b)
    return x


_drawn_inputs = setup_inputs


def setup_inputs(seed=0):
    import zlib

    import numpy as np

    out = dict(_drawn_inputs(seed))
    spreads = {}
    factors = {'L0_conv_squeeze_b': 3.107, 'L0_conv_expand1x1_b': 2.802}
    for name, (base, spread) in spreads.items():
        noise = np.random.default_rng([zlib.crc32(name.encode()), seed]).standard_normal(out[name].shape)
        drawn = base * np.exp(spread * noise) if base else spread * noise
        out[name] = jnp.asarray(drawn.astype(out[name].dtype))
    for name, factor in factors.items():
        out[name] = (out[name] * factor).astype(out[name].dtype)
    return out
```

```python
from contextlib import ExitStack

import concourse.bass as bass
from concourse import mybir

F32 = mybir.dt.float32
F32R = mybir.dt.float32r
U32 = mybir.dt.uint32
ALU = mybir.AluOpType
ACT = mybir.ActivationFunctionType

P = 128
EPS = 1e-5
GROUPS = 32
QUARTERS = 4
STATS_WIDTH = 6
NORM_STEPS = 15


def fire_kernel(nc, x, squeeze_w, squeeze_b, expand1_w, expand3_w, expand_b, group_mean, out):
    N, C, H, W = x.shape
    S = squeeze_w.shape[2]
    KC = C // P
    TAPS = expand3_w.shape[1]
    E = expand3_w.shape[2]
    MC = E // P
    ROWS = H // QUARTERS
    HALF = ROWS // 2
    QC, HCOLS = ROWS * W, HALF * W
    PW = W + 2
    PAIRS = QUARTERS * 2 * MC
    assert 2 * S == P and C == 2 * E and N % 2 == 0 and N >= 6 and HCOLS <= 512 and HCOLS % 2 == 0

    TILES = [(0, False), (MC, True), (1, False), (MC + 1, True)]

    x_v = x.rearrange("n (k p) h w -> n p k (h w)", p=P)
    out_v = out.rearrange("n (k p) h w -> n p k (h w)", p=P)

    with ExitStack() as ctx:
        def sb(name, shape, dtype=F32):
            return ctx.enter_context(nc.sbuf_tensor(name, shape, dtype))

        def sem(name):
            return ctx.enter_context(nc.semaphore(name))

        images = [sb(f"image{b}", [P, KC, H * W]) for b in range(2)]
        parts = [sb(f"parts{b}", [P, H + 2, PW], F32R) for b in range(2)]
        beside = [sb(f"beside{b}", [P, H + 2, W], F32R) for b in range(2)]
        below = [sb(f"below{b}", [P, H, W], F32R) for b in range(2)]
        squeezed = [sb(f"squeezed{b}", [P, ROWS, W + 1]) for b in range(2)]
        w3_high = sb("w3_high", [P, TAPS, E], F32R)
        w3_low_beside = sb("w3_low_beside", [P, 3, E], F32R)
        w3_low_below = sb("w3_low_below", [P, E], F32R)
        w3_low_last = sb("w3_low_last", [P, E], F32R)
        w1_high = sb("w1_high", [P, E], F32R)
        w1_low = sb("w1_low", [P, E], F32R)
        wsq_raw = sb("wsq_raw", [P, KC, S])
        wsq = sb("wsq", [P, KC, S])
        averager = sb("averager", [P, P])
        sq_bias_raw = sb("sq_bias_raw", [P, 1])
        sq_bias = sb("sq_bias", [P, 1])
        e_bias = sb("e_bias", [P, KC])
        pieces = sb("pieces", [P, KC, 2 * QUARTERS, STATS_WIDTH])
        mean_var = sb("mean_var", [P, KC, 2])
        off_mean = sb("off_mean", [P, KC])
        off_square = sb("off_square", [P, KC])
        neg_mean = sb("neg_mean", [P, KC])
        inner_var = sb("inner_var", [P, KC])
        variance = sb("variance", [P, KC])
        std = sb("std", [P, KC])
        r0 = sb("r0", [P, KC])
        r0_square = sb("r0_square", [P, KC])
        r0_miss = sb("r0_miss", [P, KC])
        r0_fix = sb("r0_fix", [P, KC])
        rstd = sb("rstd", [P, KC])

        tile_banks = [ctx.enter_context(nc.psum_tensor(f"tile{b}", [P, 2, 512], F32)) for b in range(3)]
        TILE_BANKS = [0, 1, 0, 2]
        sq_banks = [ctx.enter_context(nc.psum_tensor(f"squeeze{b}", [P, 512], F32)) for b in range(2)]
        mean_ps = sq_banks[1][:, HCOLS:HCOLS + 2 * KC].rearrange("p (k t) -> p k t", t=2)
        spread_ps = sq_banks[1][:, HCOLS + 2 * KC:HCOLS + 3 * KC]
        shift_ps = sq_banks[1][:, HCOLS + 3 * KC:HCOLS + 3 * KC + 1]

        weights_landed = sem("weights_landed")
        consts_landed = sem("consts_landed")
        landed = [[sem(f"landed{b}_{q}") for q in range(QUARTERS)] for b in range(2)]
        stored = sem("stored")
        borders_zeroed = sem("borders_zeroed")
        weights_high = sem("weights_high")
        weights_low = sem("weights_low")
        weights_ready = sem("weights_ready")
        pieces_done = sem("pieces_done")
        channels_done = sem("channels_done")
        mean_done = sem("mean_done")
        spread_done = sem("spread_done")
        norm_step = sem("norm_step")
        std_done = sem("std_done")
        shift_done = sem("shift_done")
        squeeze_done = sem("squeeze_done")
        squeezed_done = sem("squeezed_done")
        beside_done = sem("beside_done")
        parts_done = sem("parts_done")
        below_done = sem("below_done")
        tile_done = sem("tile_done")
        relu_done = sem("relu_done")
        added = sem("added")

        def wait(eng, semaphore, count):
            if not isinstance(count, int) or count > 0:
                eng.wait_ge(semaphore, count)

        def images_run(eng, period):
            for i in range(2):
                period(i, i, True, True)
            with eng.Fori(1, N // 2 - 1) as n:
                for b in range(2):
                    period(n * 2 + b, b, True, True)
            period(N - 2, 0, True, False)
            period(N - 1, 1, False, False)

        def quarter(b, q):
            return images[b][:, :, q * QC:(q + 1) * QC]

        w3_raw = images[1][:, 0, 0:TAPS * E].rearrange("p (t e) -> p t e", t=TAPS)
        w1_raw = images[1][:, 1, 0:E]

        block = ctx.enter_context(nc.Block())

        @block.sync
        def _(sp):
            def load(i, b, q):
                sp.dma_start(quarter(b, q), x_v[i, :, :, q * QC:(q + 1) * QC]).then_inc(landed[b][q], 16)

            load(0, 0, 0)
            sp.dma_start(wsq_raw[:, :, :], squeeze_w).then_inc(consts_landed, 16)
            sp.dma_start(e_bias[:, :], expand_b).then_inc(consts_landed, 16)
            sp.dma_start(averager[:, :], group_mean).then_inc(consts_landed, 16)
            for h in range(2):
                sp.dma_start(w3_raw[h * S:(h + 1) * S], expand3_w).then_inc(weights_landed, 16)
                sp.dma_start(w1_raw[h * S:(h + 1) * S], expand1_w).then_inc(weights_landed, 16)
                sp.dma_start(sq_bias_raw[h * S:(h + 1) * S], squeeze_b).then_inc(consts_landed, 16)
            for q in range(1, QUARTERS):
                load(0, 0, q)
            sp.wait_ge(weights_ready, 1)
            for q in range(QUARTERS):
                load(1, 1, q)

            def period(i, b, has_next, has_second):
                for q in range(QUARTERS):
                    wait(sp, added, i * PAIRS + 2 * MC * (q + 1))
                    sp.dma_start(out_v[i, :, :, q * QC:(q + 1) * QC], quarter(b, q)).then_inc(stored, 16)
                    wait(sp, stored, i * (16 * QUARTERS) + 16 * (q + 1))
                    if has_second:
                        load(i + 2, b, q)

            images_run(sp, period)

        @block.tensor
        def _(pe):
            def squeeze(i, b, q):
                bank = sq_banks[q % 2]
                wait(pe, squeezed_done, i * QUARTERS + q - 1)
                if q == 1:
                    wait(pe, norm_step, i * NORM_STEPS + NORM_STEPS)
                for k in range(KC):
                    for h in range(2):
                        last = pe.matmul(bank[h * S:(h + 1) * S, 0:HCOLS], wsq[:, k, :],
                                         images[b][:, k, q * QC + h * HCOLS:q * QC + (h + 1) * HCOLS],
                                         start=k == 0, stop=k == KC - 1)
                last.then_inc(squeeze_done, 1)

            def group_means(i):
                wait(pe, channels_done, i * KC + KC)
                wait(pe, squeezed_done, i * QUARTERS)
                pe.matmul(mean_ps, averager[:, :], mean_var[:, :, :], start=True, stop=True).then_inc(mean_done, 1)

            def group_spread(i):
                wait(pe, norm_step, i * NORM_STEPS + 4)
                pe.matmul(spread_ps, averager[:, :], off_square[:, :], start=True, stop=True).then_inc(spread_done, 1)

            def bias_shift(i):
                wait(pe, norm_step, i * NORM_STEPS + 14)
                for k in range(KC):
                    for h in range(2):
                        last = pe.matmul(shift_ps[h * S:(h + 1) * S], wsq[:, k, :], neg_mean[:, k:k + 1],
                                         start=k == 0, stop=k == KC - 1)
                last.then_inc(shift_done, 1)

            def passes(b, is3, m):
                cols = slice(m * P, (m + 1) * P)
                if not is3:
                    return [(w1_high[:, cols], parts[b], 1, 1), (w1_low[:, cols], parts[b], 1, 1)]
                high = [(w3_high[:, 3 * dy + dx, cols], parts[b], dy, dx) for dy in range(3) for dx in range(3)]
                low = [(w3_low_beside[:, dy, cols], beside[b], dy, 0) for dy in range(3)]
                return high + low + [(w3_low_below[:, cols], below[b], 0, 0), (w3_low_last[:, cols], parts[b], 2, 2)]

            def tile(i, b, q, t):
                chunk, is3 = TILES[t]
                banks = tile_banks[TILE_BANKS[t]]
                wait(pe, added, i * PAIRS + 2 * MC * q + t - (3 if is3 else 1))
                todo = passes(b, is3, chunk % MC)
                for n, (w, layout, r, c) in enumerate(todo):
                    for h in range(2):
                        r0 = q * ROWS + h * HALF + r
                        last = pe.matmul(banks[:, h, 0:HCOLS], w, layout[:, r0:r0 + HALF, c:c + W],
                                         start=n == 0, stop=n == len(todo) - 1)
                last.then_inc(tile_done, 1)

            def period(i, b, has_next, has_second):
                for q in range(QUARTERS):
                    wait(pe, parts_done, i * QUARTERS + min(q + 2, QUARTERS))
                    wait(pe, below_done, i * QUARTERS + min(q + 2, QUARTERS))
                    tile(i, b, q, 0)
                    tile(i, b, q, 1)
                    if has_next and q == 2:
                        group_means(i + 1)
                    if has_next and q == 3:
                        bias_shift(i + 1)
                        squeeze(i + 1, 1 - b, 0)
                        squeeze(i + 1, 1 - b, 1)
                    tile(i, b, q, 2)
                    if has_next and q == 3:
                        squeeze(i + 1, 1 - b, 2)
                        squeeze(i + 1, 1 - b, 3)
                    tile(i, b, q, 3)
                    if has_next and q == 2:
                        group_spread(i + 1)

            pe.wait_ge(consts_landed, 5 * 16)
            group_means(0)
            group_spread(0)
            bias_shift(0)
            for q in range(QUARTERS):
                squeeze(0, 0, q)
            pe.wait_ge(weights_ready, 1)
            images_run(pe, period)

        @block.scalar
        def _(act):
            def root(i):
                wait(act, norm_step, i * NORM_STEPS + 5)
                act.activation(std[:, :], variance[:, :], ACT.Sqrt).then_inc(std_done, 1)

            def unload_squeeze(i, b, q):
                to = squeezed[q % 2]
                wait(act, norm_step, i * NORM_STEPS + NORM_STEPS)
                wait(act, squeeze_done, i * QUARTERS + q + 1)
                wait(act, parts_done, i * QUARTERS + q - 1)
                wait(act, below_done, i * QUARTERS + q - 1)
                for h in range(2):
                    rows = slice(h * HALF, (h + 1) * HALF)
                    half = slice(h * S, (h + 1) * S)
                    src = sq_banks[q % 2][half, 0:HCOLS].rearrange("p (r c) -> p r c", c=W)
                    act.activation(to[0:S, rows, 1:W + 1], src, ACT.Relu, bias=sq_bias[half, :])
                    last = act.activation(to[S:P, rows, 0:W], src, ACT.Relu, bias=sq_bias[half, :])
                last.then_inc(squeezed_done, 1)
                act.wait_ge(squeezed_done, i * QUARTERS + q + 1)
                act.activation(below[b][S:P, q * ROWS:(q + 1) * ROWS, 0:W - 1],
                               to[S:P, :, 1:W], ACT.Copy).then_inc(below_done, 1)

            def relu(i, q, t):
                chunk = TILES[t][0]
                banks = tile_banks[TILE_BANKS[t]][:, :, 0:HCOLS]
                wait(act, tile_done, i * PAIRS + 2 * MC * q + t + 1)
                act.activation(banks, banks, ACT.Relu, bias=e_bias[:, chunk:chunk + 1]).then_inc(relu_done, 1)

            def period(i, b, has_next, has_second):
                for q in range(QUARTERS):
                    relu(i, q, 0)
                    relu(i, q, 1)
                    if has_next and q == 3:
                        unload_squeeze(i + 1, 1 - b, 0)
                        unload_squeeze(i + 1, 1 - b, 1)
                    relu(i, q, 2)
                    if has_next and q == 2:
                        root(i + 1)
                    if has_next and q == 3:
                        unload_squeeze(i + 1, 1 - b, 2)
                        unload_squeeze(i + 1, 1 - b, 3)
                    relu(i, q, 3)

            act.wait_ge(weights_landed, 4 * 16)
            act.activation(w3_high[:, :, :], w3_raw, ACT.Copy)
            act.activation(w1_high[:, :], w1_raw, ACT.Copy).then_inc(weights_high, 1)
            act.wait_ge(consts_landed, 5 * 16)
            root(0)
            act.wait_ge(borders_zeroed, 1)
            for q in range(QUARTERS):
                unload_squeeze(0, 0, q)
            images_run(act, period)

        @block.gpsimd
        def _(pool):
            for b in range(2):
                for tensor in (parts[b], beside[b]):
                    for row in (0, H + 1):
                        pool.memset(tensor[:, row, :].bitcast(U32), 0)
                for col in (0, PW - 1):
                    pool.memset(parts[b][:, 1:H + 1, col:col + 1].bitcast(U32), 0)
                pool.memset(below[b][:, :, W - 1:W].bitcast(U32), 0)
                pool.memset(below[b][:, 0, 0:W - 1].bitcast(U32), 0)
                pool.memset(squeezed[b][:, :, 0:1], 0.0)
                last = pool.memset(squeezed[b][:, :, W:W + 1], 0.0)
            last.then_inc(borders_zeroed, 1)

            def low(dst, raw, high):
                return pool.tensor_tensor(dst, raw, high.bitcast(F32), ALU.subtract)

            pool.wait_ge(weights_high, 1)
            for h in range(2):
                half = slice(h * S, (h + 1) * S)
                for dy in range(3):
                    low(w3_low_beside[half, dy, :], w3_raw[half, 3 * dy + h, :], w3_high[half, 3 * dy + h, :])
                low(w3_low_below[half, :], w3_raw[half, 3 * h + 2, :],
                    w3_high[half, 3 * h + 2, :]).then_inc(weights_low, 1)
                pool.wait_ge(weights_low, h + 1)
            low(w3_low_last[:, :], w3_raw[:, TAPS - 1, :], w3_high[:, TAPS - 1, :])
            low(w1_low[:, :], w1_raw, w1_high[:, :]).then_inc(weights_ready, 1)

        @block.vector
        def _(dve):
            def statistics(i, b, q, k):
                if k == 0:
                    wait(dve, landed[b][q], (i - b) * 8 + 16)
                    wait(dve, channels_done, i * KC)
                for h in range(2):
                    cols = slice(q * QC + h * HCOLS, q * QC + (h + 1) * HCOLS)
                    dve.bn_stats(pieces[:, k, 2 * q + h, :], images[b][:, k, cols]).then_inc(pieces_done, 1)

            def pieces_wait(i):
                wait(dve, pieces_done, i * (2 * QUARTERS * KC) + 2 * QUARTERS * KC)
                wait(dve, mean_done, i)

            def channel_statistics(i):
                for k in range(KC):
                    dve.bn_aggr(mean_var[:, k, :], pieces[:, k, :, :]).then_inc(channels_done, 1)

            def step(i, n, instruction, then_wait=False):
                instruction.then_inc(norm_step, 1)
                if then_wait:
                    wait(dve, norm_step, i * NORM_STEPS + n)

            def norm_means(i):
                wait(dve, mean_done, i + 1)
                wait(dve, channels_done, i * KC + KC)
                wait(dve, shift_done, i)
                step(i, 1, dve.tensor_tensor(off_mean[:, :], mean_var[:, :, 0], mean_ps[:, :, 0], ALU.subtract))
                step(i, 2, dve.tensor_scalar(neg_mean[:, :], mean_ps[:, :, 0], -1.0, None, ALU.mult))
                step(i, 3, dve.tensor_scalar(inner_var[:, :], mean_ps[:, :, 1], EPS, None, ALU.add), True)
                step(i, 4, dve.tensor_tensor(off_square[:, :], off_mean[:, :], off_mean[:, :], ALU.mult))

            def norm_variance(i):
                wait(dve, spread_done, i + 1)
                wait(dve, norm_step, i * NORM_STEPS + 4)
                step(i, 5, dve.tensor_tensor(variance[:, :], inner_var[:, :], spread_ps, ALU.add), True)

            def norm_weights(i):
                wait(dve, std_done, i + 1)
                step(i, 6, dve.reciprocal(r0[:, :], std[:, :]), True)
                step(i, 7, dve.tensor_tensor(r0_square[:, :], r0[:, :], r0[:, :], ALU.mult), True)
                step(i, 8, dve.tensor_tensor(r0_miss[:, :], r0_square[:, :], variance[:, :], ALU.mult), True)
                step(i, 9, dve.tensor_scalar(r0_fix[:, :], r0_miss[:, :], -0.5, 1.5, ALU.mult, ALU.add), True)
                step(i, 10, dve.tensor_tensor(rstd[:, :], r0[:, :], r0_fix[:, :], ALU.mult), True)
                wait(dve, squeeze_done, i * QUARTERS)
                for k in range(KC):
                    step(i, 11 + k, dve.tensor_scalar(wsq[:, k, :], wsq_raw[:, k, :], rstd[:, k:k + 1], None, ALU.mult))

            def norm_bias(i):
                wait(dve, shift_done, i + 1)
                wait(dve, squeezed_done, i * QUARTERS)
                step(i, 15, dve.tensor_tensor(sq_bias[:, :], sq_bias_raw[:, :], shift_ps, ALU.add))

            def split(i, b, q):
                src = squeezed[q % 2]
                rows = slice(q * ROWS + 1, (q + 1) * ROWS + 1)
                wait(dve, squeezed_done, i * QUARTERS + q + 1)
                dve.tensor_copy(beside[b][:, rows, :], src[:, :, 0:W]).then_inc(beside_done, 1)
                dve.tensor_copy(parts[b][0:S, rows, 1:W + 1], src[0:S, :, 1:W + 1])
                n = ROWS if q < QUARTERS - 1 else ROWS - 1
                dve.tensor_copy(below[b][0:S, q * ROWS + 1:q * ROWS + 1 + n, 0:W - 1], src[0:S, 0:n, 2:W + 1])
                wait(dve, beside_done, i * QUARTERS + q + 1)
                dve.tensor_tensor(parts[b][S:P, rows, 1:W + 1], src[S:P, :, 0:W],
                                  beside[b][S:P, rows, :].bitcast(F32), ALU.subtract).then_inc(parts_done, 1)

            def add(i, b, q, t):
                chunk = TILES[t][0]
                res = images[b][:, chunk, q * QC:(q + 1) * QC].rearrange("p (h c) -> p h c", h=2)
                wait(dve, relu_done, i * PAIRS + 2 * MC * q + t + 1)
                dve.tensor_tensor(res, tile_banks[TILE_BANKS[t]][:, :, 0:HCOLS], res, ALU.add).then_inc(added, 1)

            def period(i, b, has_next, has_second):
                for q in range(QUARTERS):
                    for t in range(len(TILES)):
                        if has_next and (q, t) == (2, 0):
                            pieces_wait(i + 1)
                        if has_next and (q, t) == (2, 3):
                            norm_variance(i + 1)
                            norm_weights(i + 1)
                        add(i, b, q, t)
                        if has_next and (q, t) == (2, 0):
                            channel_statistics(i + 1)
                        if has_next and (q, t) == (2, 1):
                            norm_means(i + 1)
                        if has_next and (q, t) == (3, 1):
                            norm_bias(i + 1)
                        if has_next and q < 2:
                            statistics(i + 1, 1 - b, q + 2, t)
                        if has_second and q >= 2:
                            statistics(i + 2, b, q - 2, t)
                        if has_next and (q, t) == (3, 1):
                            split(i + 1, 1 - b, 0)
                            split(i + 1, 1 - b, 1)
                        if has_next and (q, t) == (3, 2):
                            split(i + 1, 1 - b, 2)
                            split(i + 1, 1 - b, 3)

            dve.wait_ge(consts_landed, 5 * 16)
            for q in range(QUARTERS):
                for k in range(KC):
                    statistics(0, 0, q, k)
            pieces_wait(0)
            channel_statistics(0)
            norm_means(0)
            norm_variance(0)
            norm_weights(0)
            norm_bias(0)
            for q in range(QUARTERS):
                split(0, 0, q)
            for q in range(2):
                for k in range(KC):
                    statistics(1, 1, q, k)
            images_run(dve, period)


def kernel(x, L0_conv_squeeze_w, L0_conv_squeeze_b, L0_conv_expand1x1_w, L0_conv_expand1x1_b,
           L0_conv_expand3x3_w, L0_conv_expand3x3_b):
    import numpy as np
    import concourse.bacc as bacc
    from concourse.bass_utils import run_bass_kernel_spmd

    x = np.ascontiguousarray(x)
    sq_w, w1, w3 = (np.asarray(a) for a in (L0_conv_squeeze_w, L0_conv_expand1x1_w, L0_conv_expand3x3_w))
    channels = x.shape[1]
    squeezed = sq_w.shape[0]
    per_group = channels // GROUPS
    same_group = np.kron(np.eye(P // per_group), np.ones((per_group, per_group)))
    bias = np.concatenate([np.asarray(L0_conv_expand1x1_b), np.asarray(L0_conv_expand3x3_b)])
    arrays = {
        "x": x,
        "squeeze_w": sq_w.T.reshape(channels // P, P, squeezed).transpose(1, 0, 2),
        "squeeze_b": np.asarray(L0_conv_squeeze_b).reshape(squeezed, 1),
        "expand1_w": w1.T,
        "expand3_w": w3.reshape(w3.shape[0], squeezed, -1).transpose(1, 2, 0),
        "expand_b": bias.reshape(channels // P, P).T,
        "group_mean": (same_group / per_group).astype(np.float32),
    }
    arrays = {name: np.ascontiguousarray(a) for name, a in arrays.items()}
    nc = bacc.Bacc("TRN2", target_bir_lowering=False, num_devices=1)
    args = [nc.dram_tensor(f"{name}_dram", a.shape, mybir.dt.from_np(a.dtype), kind="ExternalInput").ap()
            for name, a in arrays.items()]
    args.append(nc.dram_tensor("out_dram", x.shape, mybir.dt.from_np(x.dtype), kind="ExternalOutput").ap())
    fire_kernel(nc, *args)
    run = run_bass_kernel_spmd(nc, [{f"{name}_dram": a for name, a in arrays.items()}], core_ids=[0])
    return run.results[0]["out_dram"]
```

```python
from contextlib import ExitStack

import concourse.bass as bass
from concourse import mybir

F32 = mybir.dt.float32
F32R = mybir.dt.float32r
U32 = mybir.dt.uint32
ALU = mybir.AluOpType
ACT = mybir.ActivationFunctionType

P = 128
EPS = 1e-5
GROUPS = 32
QUARTERS = 4
STATS_WIDTH = 6
NORM_STEPS = 19


def fire_kernel(nc, x, squeeze_w, squeeze_b, expand1_w, expand3_w, expand_b, group_mean, out):
    N, C, H, W = x.shape
    S = squeeze_b.shape[0]
    KC = C // P
    KS = 3
    E = expand1_w.shape[1]
    MC = E // P
    ROWS = H // QUARTERS
    HALF = ROWS // 2
    QC, HCOLS = ROWS * W, HALF * W
    PW = W + 2
    PAIRS = QUARTERS * 2 * MC
    assert 2 * S == P and C == 2 * E and N % 2 == 0 and N >= 6 and HCOLS <= 512 and HCOLS % 2 == 0

    TILES = [(0, False), (MC, True), (1, False), (MC + 1, True)]

    x_v = x.rearrange("n (k p) h w -> n p k (h w)", p=P)
    out_v = out.rearrange("n (k p) h w -> n p k (h w)", p=P)

    with ExitStack() as ctx:
        def sb(name, shape, dtype=F32):
            return ctx.enter_context(nc.sbuf_tensor(name, shape, dtype))

        def sem(name):
            return ctx.enter_context(nc.semaphore(name))

        images = [sb(f"image{b}", [P, KC, H * W]) for b in range(2)]
        parts = [sb(f"parts{b}", [P, H + 2, PW], F32R) for b in range(2)]
        beside = [sb(f"beside{b}", [P, H + 2, W], F32R) for b in range(2)]
        below = [sb(f"below{b}", [P, H, W], F32R) for b in range(2)]
        squeezed = [sb(f"squeezed{b}", [P, ROWS, W + 1]) for b in range(2)]
        w3_high = sb("w3_high", [P, KS, KS * E], F32R)
        w3_low_beside = sb("w3_low_beside", [P, KS, E], F32R)
        w3_low_below = sb("w3_low_below", [P, E], F32R)
        w3_low_last = sb("w3_low_last", [P, E], F32R)
        w1_high = sb("w1_high", [P, E], F32R)
        w1_low = sb("w1_low", [P, E], F32R)
        wsq_raw = sb("wsq_raw", [P, KC, P])
        wsq = sb("wsq", [P, KC, P])
        shift_terms = sb("shift_terms", [P, P])
        ones = sb("ones", [P, 1])
        averager = sb("averager", [P, P])
        sq_bias_raw = sb("sq_bias_raw", [P, 1])
        sq_bias = sb("sq_bias", [P, 1])
        e_bias = sb("e_bias", [P, KC])
        pieces = sb("pieces", [P, KC, 2 * QUARTERS, STATS_WIDTH])
        mean_var = sb("mean_var", [P, KC, 2])
        off_mean = sb("off_mean", [P, KC])
        off_square = sb("off_square", [P, KC])
        neg_mean = sb("neg_mean", [P, KC])
        inner_var = sb("inner_var", [P, KC])
        variance = sb("variance", [P, KC])
        std = sb("std", [P, KC])
        r0 = sb("r0", [P, KC])
        r0_square = sb("r0_square", [P, KC])
        r0_miss = sb("r0_miss", [P, KC])
        r0_fix = sb("r0_fix", [P, KC])
        rstd = sb("rstd", [P, KC])

        tile_banks = [ctx.enter_context(nc.psum_tensor(f"tile{b}", [P, 2, 512], F32)) for b in range(3)]
        TILE_BANKS = [0, 1, 0, 2]
        sq_banks = [ctx.enter_context(nc.psum_tensor(f"squeeze{b}", [P, 512], F32)) for b in range(2)]
        mean_ps = sq_banks[1][:, HCOLS:HCOLS + 2 * KC].rearrange("p (k t) -> p k t", t=2)
        spread_ps = sq_banks[1][:, HCOLS + 2 * KC:HCOLS + 3 * KC]
        shift_ps = sq_banks[1][:, HCOLS + 3 * KC:HCOLS + 3 * KC + 1]

        weights_landed = sem("weights_landed")
        consts_landed = sem("consts_landed")
        landed = [[sem(f"landed{b}_{q}") for q in range(QUARTERS)] for b in range(2)]
        landed_early = sem("landed_early")
        stored = [[sem(f"stored{b}_{q}") for q in range(QUARTERS)] for b in range(2)]
        ones_set = sem("ones_set")
        stored_last = sem("stored_last")
        borders_zeroed = sem("borders_zeroed")
        weights_high = sem("weights_high")
        weights_low = sem("weights_low")
        weights_ready = sem("weights_ready")
        pieces_done = sem("pieces_done")
        channels_done = sem("channels_done")
        mean_done = sem("mean_done")
        spread_done = sem("spread_done")
        norm_step = sem("norm_step")
        std_done = sem("std_done")
        shift_done = sem("shift_done")
        squeeze_done = sem("squeeze_done")
        squeezed_done = sem("squeezed_done")
        beside_done = sem("beside_done")
        parts_done = sem("parts_done")
        below_done = sem("below_done")
        tile_done = sem("tile_done")
        relu_done = sem("relu_done")
        added = sem("added")

        def wait(eng, semaphore, count):
            if not isinstance(count, int) or count > 0:
                eng.wait_ge(semaphore, count)

        def images_run(eng, period):
            period(0, 0, True, True, first=True)
            period(1, 1, True, True)
            with nc.Fori(1, N // 2 - 1, engines=bass.OrderedEngineSet([eng.engine]), hint_back_edge=True) as n:
                for b in range(2):
                    period(n * 2 + b, b, True, True)
            period(N - 2, 0, True, False)
            period(N - 1, 1, False, False)

        def quarter(b, q):
            return images[b][:, :, q * QC:(q + 1) * QC]

        w3_raw = quarter(1, QUARTERS - 1)[:, 0:KS, 0:KS * E]
        w1_raw = quarter(1, QUARTERS - 1)[:, KS, 0:E]

        block = ctx.enter_context(nc.Block())

        @block.sync
        def _(sp):
            def load(i, b, q):
                sp.dma_start(quarter(b, q), x_v[i, :, :, q * QC:(q + 1) * QC]).then_inc(landed[b][q], 16)

            for q in range(QUARTERS - 1):
                load(0, 0, q)
            for chunks, there in ((slice(0, KC // 2), landed_early), (slice(KC // 2, KC), landed[0][QUARTERS - 1])):
                sp.dma_start(quarter(0, QUARTERS - 1)[:, chunks, :],
                             x_v[0, :, chunks, (QUARTERS - 1) * QC:QUARTERS * QC]).then_inc(there, 16)
            sp.dma_start(wsq_raw[:, :, :], squeeze_w).then_inc(consts_landed, 16)
            sp.dma_start(e_bias[:, :], expand_b).then_inc(consts_landed, 16)
            sp.dma_start(averager[:, :], group_mean).then_inc(consts_landed, 16)
            for h in range(2):
                sp.dma_start(sq_bias_raw[h * S:(h + 1) * S], squeeze_b).then_inc(consts_landed, 16)
            for h in range(2):
                sp.dma_start(w3_raw[h * S:(h + 1) * S], expand3_w).then_inc(weights_landed, 16)
                sp.dma_start(w1_raw[h * S:(h + 1) * S], expand1_w).then_inc(weights_landed, 16)
            for q in range(QUARTERS):
                if q == QUARTERS - 1:
                    sp.wait_ge(weights_ready, 1)
                load(1, 1, q)

            def period(i, b, has_next, has_second, first=False):
                if has_second:
                    for q in range(QUARTERS):
                        wait(sp, stored[b][q], (i - b) * 8 + 16)
                        load(i + 2, b, q)

            images_run(sp, period)
            for b in range(2):
                for q in range(QUARTERS):
                    of_tiles = b == 1 and q == QUARTERS - 1
                    sp.wait_ge(stored[b][q], 16 * (N // 2 - of_tiles))
            sp.wait_ge(stored_last, 16 * len(TILES))

        @block.tensor
        def _(pe):
            def squeeze(i, b, q):
                bank = sq_banks[q % 2]
                wait(pe, squeezed_done, i * QUARTERS + q - 1)
                if q == 1:
                    wait(pe, norm_step, i * NORM_STEPS + NORM_STEPS)
                for k in range(KC):
                    for h in range(2):
                        last = pe.matmul(bank[h * S:(h + 1) * S, 0:HCOLS], wsq[:, k, 0:S],
                                         images[b][:, k, q * QC + h * HCOLS:q * QC + (h + 1) * HCOLS],
                                         start=k == 0, stop=k == KC - 1)
                last.then_inc(squeeze_done, 1)

            def group_means(i):
                wait(pe, channels_done, i * KC + KC)
                wait(pe, squeezed_done, i * QUARTERS)
                pe.matmul(mean_ps, averager[:, :], mean_var[:, :, :], start=True, stop=True).then_inc(mean_done, 1)

            def group_spread(i):
                wait(pe, norm_step, i * NORM_STEPS + 4)
                pe.matmul(spread_ps, averager[:, :], off_square[:, :], start=True, stop=True).then_inc(spread_done, 1)

            def bias_shift(i):
                wait(pe, norm_step, i * NORM_STEPS + 18)
                pe.matmul(shift_ps, shift_terms[:, :], ones[:, :], start=True, stop=True).then_inc(shift_done, 1)

            def passes(b, is3, m):
                cols = slice(m * P, (m + 1) * P)
                if not is3:
                    return [(w1_high[:, cols], parts[b], 1, 1), (w1_low[:, cols], parts[b], 1, 1)]
                high = [(w3_high[:, dy, dx * E + m * P:dx * E + (m + 1) * P], parts[b], dy, dx)
                        for dy in range(KS) for dx in range(KS)]
                low = [(w3_low_beside[:, dy, cols], beside[b], dy, 0) for dy in range(KS)]
                return high + low + [(w3_low_below[:, cols], below[b], 0, 0), (w3_low_last[:, cols], parts[b], 2, 2)]

            def tile(i, b, q, t):
                chunk, is3 = TILES[t]
                banks = tile_banks[TILE_BANKS[t]]
                wait(pe, added, i * PAIRS + 2 * MC * q + t - (3 if is3 else 1))
                todo = passes(b, is3, chunk % MC)
                for n, (w, layout, r, c) in enumerate(todo):
                    for h in range(2):
                        r0 = q * ROWS + h * HALF + r
                        last = pe.matmul(banks[:, h, 0:HCOLS], w, layout[:, r0:r0 + HALF, c:c + W],
                                         start=n == 0, stop=n == len(todo) - 1)
                last.then_inc(tile_done, 1)

            def period(i, b, has_next, has_second, first=False):
                for q in range(QUARTERS):
                    wait(pe, parts_done, i * QUARTERS + min(q + 2, QUARTERS))
                    wait(pe, below_done, i * QUARTERS + min(q + 2, QUARTERS))
                    tile(i, b, q, 0)
                    tile(i, b, q, 1)
                    if has_next and q == 2:
                        group_means(i + 1)
                    if has_next and q == 3:
                        bias_shift(i + 1)
                        squeeze(i + 1, 1 - b, 0)
                        squeeze(i + 1, 1 - b, 1)
                    tile(i, b, q, 2)
                    if has_next and q == 3:
                        squeeze(i + 1, 1 - b, 2)
                        squeeze(i + 1, 1 - b, 3)
                    tile(i, b, q, 3)
                    if has_next and q == 2:
                        group_spread(i + 1)

            pe.wait_ge(consts_landed, 5 * 16)
            group_means(0)
            group_spread(0)
            pe.wait_ge(ones_set, 1)
            bias_shift(0)
            for q in range(QUARTERS):
                squeeze(0, 0, q)
            pe.wait_ge(weights_ready, 1)
            images_run(pe, period)

        @block.scalar
        def _(act):
            def root(i):
                wait(act, norm_step, i * NORM_STEPS + 5)
                act.activation(std[:, :], variance[:, :], ACT.Sqrt).then_inc(std_done, 1)

            def unload_squeeze(i, b, q):
                to = squeezed[q % 2]
                wait(act, norm_step, i * NORM_STEPS + NORM_STEPS)
                wait(act, squeeze_done, i * QUARTERS + q + 1)
                wait(act, parts_done, i * QUARTERS + q - 1)
                wait(act, below_done, i * QUARTERS + q - 1)
                for h in range(2):
                    rows = slice(h * HALF, (h + 1) * HALF)
                    half = slice(h * S, (h + 1) * S)
                    src = sq_banks[q % 2][half, 0:HCOLS].rearrange("p (r c) -> p r c", c=W)
                    act.activation(to[0:S, rows, 1:W + 1], src, ACT.Relu, bias=sq_bias[half, :])
                    last = act.activation(to[S:P, rows, 0:W], src, ACT.Relu, bias=sq_bias[half, :])
                last.then_inc(squeezed_done, 1)
                act.wait_ge(squeezed_done, i * QUARTERS + q + 1)
                act.activation(below[b][S:P, q * ROWS:(q + 1) * ROWS, 0:W - 1],
                               to[S:P, :, 1:W], ACT.Copy).then_inc(below_done, 1)

            def relu(i, q, t):
                chunk = TILES[t][0]
                banks = tile_banks[TILE_BANKS[t]][:, :, 0:HCOLS]
                wait(act, tile_done, i * PAIRS + 2 * MC * q + t + 1)
                act.activation(banks, banks, ACT.Relu, bias=e_bias[:, chunk:chunk + 1]).then_inc(relu_done, 1)

            def store(i, b, q):
                wait(act, added, i * PAIRS + 2 * MC * (q + 1))
                act.dma_start(out_v[i, :, :, q * QC:(q + 1) * QC], quarter(b, q)).then_inc(stored[b][q], 16)

            def store_tile(i, b, q, t):
                chunk, cols = TILES[t][0], slice(q * QC, (q + 1) * QC)
                wait(act, added, i * PAIRS + 2 * MC * q + t + 1)
                act.dma_start(out_v[i, :, chunk, cols], images[b][:, chunk, cols]).then_inc(stored_last, 16)

            def period(i, b, has_next, has_second, first=False):
                for q in range(QUARTERS):
                    relu(i, q, 0)
                    if q > 0:
                        store(i, b, q - 1)
                    elif not first:
                        store(i - 1, 1 - b, QUARTERS - 1)
                    if not has_next and q == QUARTERS - 1:
                        for t in range(1, len(TILES)):
                            relu(i, q, t)
                            store_tile(i, b, q, t - 1)
                        store_tile(i, b, q, len(TILES) - 1)
                        break
                    relu(i, q, 1)
                    if has_next and q == 3:
                        unload_squeeze(i + 1, 1 - b, 0)
                        unload_squeeze(i + 1, 1 - b, 1)
                    relu(i, q, 2)
                    if has_next and q == 2:
                        root(i + 1)
                    if has_next and q == 3:
                        unload_squeeze(i + 1, 1 - b, 2)
                        unload_squeeze(i + 1, 1 - b, 3)
                    relu(i, q, 3)

            root(0)
            act.wait_ge(consts_landed, 5 * 16)
            act.wait_ge(borders_zeroed, 1)
            for q in range(QUARTERS):
                unload_squeeze(0, 0, q)
            images_run(act, period)

        @block.gpsimd
        def _(pool):
            for b in range(2):
                for tensor in (parts[b], beside[b]):
                    for row in (0, H + 1):
                        pool.memset(tensor[:, row, :].bitcast(U32), 0)
                for col in (0, PW - 1):
                    pool.memset(parts[b][:, 1:H + 1, col:col + 1].bitcast(U32), 0)
                pool.memset(below[b][:, :, W - 1:W].bitcast(U32), 0)
                pool.memset(below[b][:, 0, 0:W - 1].bitcast(U32), 0)
                pool.memset(squeezed[b][:, :, 0:1], 0.0)
                last = pool.memset(squeezed[b][:, :, W:W + 1], 0.0)
            last.then_inc(borders_zeroed, 1)
            pool.memset(ones[:, :], 1.0).then_inc(ones_set, 1)

            pool.wait_ge(weights_landed, 4 * 16)
            pool.tensor_copy(w3_high[:, :, :], w3_raw)
            pool.tensor_copy(w1_high[:, :], w1_raw).then_inc(weights_high, 1)

            def low(dst, raw, high):
                return pool.tensor_tensor(dst, raw, high.bitcast(F32), ALU.subtract)

            pool.wait_ge(weights_high, 1)
            for h in range(2):
                half = slice(h * S, (h + 1) * S)
                tap = slice(h * E, (h + 1) * E)
                low(w3_low_beside[half, :, :], w3_raw[half, :, tap], w3_high[half, :, tap])
                low(w3_low_below[half, :], w3_raw[half, h, 2 * E:], w3_high[half, h, 2 * E:]).then_inc(weights_low, 1)
                pool.wait_ge(weights_low, h + 1)
            low(w3_low_last[:, :], w3_raw[:, KS - 1, 2 * E:], w3_high[:, KS - 1, 2 * E:])
            low(w1_low[:, :], w1_raw, w1_high[:, :]).then_inc(weights_ready, 1)

        @block.vector
        def _(dve):
            def statistics(i, b, q, k):
                if k == 0:
                    wait(dve, landed[b][q], (i - b) * 8 + 16)
                    wait(dve, channels_done, i * KC)
                pieces_of(b, q, k)

            def pieces_of(b, q, k):
                for h in range(2):
                    cols = slice(q * QC + h * HCOLS, q * QC + (h + 1) * HCOLS)
                    dve.bn_stats(pieces[:, k, 2 * q + h, :], images[b][:, k, cols]).then_inc(pieces_done, 1)

            def pieces_wait(i):
                wait(dve, pieces_done, i * (2 * QUARTERS * KC) + 2 * QUARTERS * KC)
                wait(dve, mean_done, i)

            def channel_statistics(i):
                for k in range(KC):
                    dve.bn_aggr(mean_var[:, k, :], pieces[:, k, :, :]).then_inc(channels_done, 1)

            def step(i, n, instruction, then_wait=False):
                instruction.then_inc(norm_step, 1)
                if then_wait:
                    wait(dve, norm_step, i * NORM_STEPS + n)

            def norm_means(i):
                wait(dve, mean_done, i + 1)
                wait(dve, channels_done, i * KC + KC)
                step(i, 1, dve.tensor_tensor(off_mean[:, :], mean_var[:, :, 0], mean_ps[:, :, 0], ALU.subtract))
                step(i, 2, dve.tensor_scalar(neg_mean[:, :], mean_ps[:, :, 0], -1.0, None, ALU.mult))
                step(i, 3, dve.tensor_scalar(inner_var[:, :], mean_ps[:, :, 1], EPS, None, ALU.add), True)
                step(i, 4, dve.tensor_tensor(off_square[:, :], off_mean[:, :], off_mean[:, :], ALU.mult))

            def norm_variance(i):
                wait(dve, spread_done, i + 1)
                wait(dve, norm_step, i * NORM_STEPS + 4)
                step(i, 5, dve.tensor_tensor(variance[:, :], inner_var[:, :], spread_ps, ALU.add), True)

            def norm_weights(i):
                wait(dve, std_done, i + 1)
                step(i, 6, dve.reciprocal(r0[:, :], std[:, :]), True)
                step(i, 7, dve.tensor_tensor(r0_square[:, :], r0[:, :], r0[:, :], ALU.mult), True)
                step(i, 8, dve.tensor_tensor(r0_miss[:, :], r0_square[:, :], variance[:, :], ALU.mult), True)
                step(i, 9, dve.tensor_scalar(r0_fix[:, :], r0_miss[:, :], -0.5, 1.5, ALU.mult, ALU.add), True)
                step(i, 10, dve.tensor_tensor(rstd[:, :], r0[:, :], r0_fix[:, :], ALU.mult), True)
                wait(dve, squeeze_done, i * QUARTERS)
                for k in range(KC):
                    step(i, 11 + k, dve.tensor_scalar(wsq[:, k, :], wsq_raw[:, k, :], rstd[:, k:k + 1], None, ALU.mult))

            def norm_shift(i):
                wait(dve, norm_step, i * NORM_STEPS + 14)
                wait(dve, shift_done, i)
                step(i, 15, dve.tensor_scalar(shift_terms[:, :], wsq[:, 0, :], neg_mean[:, 0:1], None, ALU.mult), True)
                for k in range(1, KC):
                    step(i, 15 + k, dve.scalar_tensor_tensor(shift_terms[:, :], wsq[:, k, :], neg_mean[:, k:k + 1],
                                                             shift_terms[:, :], ALU.mult, ALU.add), True)

            def norm_bias(i):
                wait(dve, shift_done, i + 1)
                wait(dve, squeezed_done, i * QUARTERS)
                step(i, 19, dve.tensor_tensor(sq_bias[:, :], sq_bias_raw[:, :], shift_ps, ALU.add))

            def split(i, b, q):
                src = squeezed[q % 2]
                rows = slice(q * ROWS + 1, (q + 1) * ROWS + 1)
                wait(dve, squeezed_done, i * QUARTERS + q + 1)
                dve.tensor_copy(beside[b][:, rows, :], src[:, :, 0:W]).then_inc(beside_done, 1)
                dve.tensor_copy(parts[b][0:S, rows, 1:W + 1], src[0:S, :, 1:W + 1])
                n = ROWS if q < QUARTERS - 1 else ROWS - 1
                dve.tensor_copy(below[b][0:S, q * ROWS + 1:q * ROWS + 1 + n, 0:W - 1], src[0:S, 0:n, 2:W + 1])
                wait(dve, beside_done, i * QUARTERS + q + 1)
                dve.tensor_tensor(parts[b][S:P, rows, 1:W + 1], src[S:P, :, 0:W],
                                  beside[b][S:P, rows, :].bitcast(F32), ALU.subtract).then_inc(parts_done, 1)

            def add(i, b, q, t):
                chunk = TILES[t][0]
                res = images[b][:, chunk, q * QC:(q + 1) * QC].rearrange("p (h c) -> p h c", h=2)
                wait(dve, relu_done, i * PAIRS + 2 * MC * q + t + 1)
                dve.tensor_tensor(res, tile_banks[TILE_BANKS[t]][:, :, 0:HCOLS], res, ALU.add).then_inc(added, 1)

            def period(i, b, has_next, has_second, first=False):
                for q in range(QUARTERS):
                    for t in range(len(TILES)):
                        if has_next and (q, t) == (2, 0):
                            pieces_wait(i + 1)
                        if has_next and (q, t) == (2, 3):
                            norm_variance(i + 1)
                            norm_weights(i + 1)
                            norm_shift(i + 1)
                        if has_next and (q, t) == (3, 1):
                            norm_bias(i + 1)
                        add(i, b, q, t)
                        if has_next and (q, t) == (2, 0):
                            channel_statistics(i + 1)
                        if has_next and (q, t) == (2, 1):
                            norm_means(i + 1)
                        if first and q < 2:
                            statistics(1, 1, q, t)
                        if has_next and q < 2:
                            statistics(i + 1, 1 - b, q + 2, t)
                        if has_second and q >= 2:
                            statistics(i + 2, b, q - 2, t)
                        if has_next and (q, t) == (3, 1):
                            split(i + 1, 1 - b, 0)
                            split(i + 1, 1 - b, 1)
                        if has_next and (q, t) == (3, 2):
                            split(i + 1, 1 - b, 2)
                            split(i + 1, 1 - b, 3)

            for q in range(QUARTERS - 1):
                for k in range(KC):
                    statistics(0, 0, q, k)
            for k in range(KC):
                if k == 0:
                    dve.wait_ge(landed_early, 16)
                if k == KC // 2:
                    dve.wait_ge(landed[0][QUARTERS - 1], 16)
                pieces_of(0, QUARTERS - 1, k)
            pieces_wait(0)
            channel_statistics(0)
            norm_means(0)
            norm_variance(0)
            dve.wait_ge(consts_landed, 5 * 16)
            norm_weights(0)
            norm_shift(0)
            norm_bias(0)
            for q in range(QUARTERS):
                split(0, 0, q)
            images_run(dve, period)


def kernel(x, L0_conv_squeeze_w, L0_conv_squeeze_b, L0_conv_expand1x1_w, L0_conv_expand1x1_b,
           L0_conv_expand3x3_w, L0_conv_expand3x3_b):
    import numpy as np
    import concourse.bacc as bacc
    from concourse.bass_utils import run_bass_kernel_spmd

    x = np.ascontiguousarray(x)
    sq_w, w1, w3 = (np.asarray(a) for a in (L0_conv_squeeze_w, L0_conv_expand1x1_w, L0_conv_expand3x3_w))
    channels = x.shape[1]
    squeezed = sq_w.shape[0]
    per_group = channels // GROUPS
    same_group = np.kron(np.eye(P // per_group), np.ones((per_group, per_group)))
    bias = np.concatenate([np.asarray(L0_conv_expand1x1_b), np.asarray(L0_conv_expand3x3_b)])
    arrays = {
        "x": x,
        "squeeze_w": np.tile(sq_w.T.reshape(channels // P, P, squeezed).transpose(1, 0, 2), (1, 1, P // squeezed)),
        "squeeze_b": np.asarray(L0_conv_squeeze_b).reshape(squeezed, 1),
        "expand1_w": w1.T,
        "expand3_w": w3.transpose(1, 2, 3, 0).reshape(squeezed, w3.shape[2], -1),
        "expand_b": bias.reshape(channels // P, P).T,
        "group_mean": (same_group / per_group).astype(np.float32),
    }
    arrays = {name: np.ascontiguousarray(a) for name, a in arrays.items()}
    nc = bacc.Bacc("TRN2", target_bir_lowering=False, num_devices=1)
    args = [nc.dram_tensor(f"{name}_dram", a.shape, mybir.dt.from_np(a.dtype), kind="ExternalInput").ap()
            for name, a in arrays.items()]
    args.append(nc.dram_tensor("out_dram", x.shape, mybir.dt.from_np(x.dtype), kind="ExternalOutput").ap())
    fire_kernel(nc, *args)
    run = run_bass_kernel_spmd(nc, [{f"{name}_dram": a for name, a in arrays.items()}], core_ids=[0])
    return run.results[0]["out_dram"]
```
